# Optimizing a Trainium2 kernel written in Bass

```python
import numpy as np
import jax
import jax.numpy as jnp

def _softmax(x, axis=-1):
    return jax.nn.softmax(x, axis=axis)

def _gelu(x):
    return jax.nn.gelu(x, approximate=True)

def _silu(x):
    return jax.nn.silu(x)

def _sigmoid(x):
    return jax.nn.sigmoid(x)

def _layernorm(x, axis=-1, eps=1e-05):
    m = jnp.mean(x, axis=axis, keepdims=True)
    v = jnp.var(x, axis=axis, keepdims=True)
    return (x - m) / jnp.sqrt(v + eps)

def _scatter_add(tgt, idx, src, axis=0):
    return tgt.at[idx].add(src)

def _segment_sum(src, seg, n):
    return jax.ops.segment_sum(src, seg, n)
kernel_name = 'mk_vit_tower_postln_d1_tok_img768_r4_3fc21f'

def setup_inputs(seed: int=0):
    np.random.seed(seed)
    _w = jnp.asarray

    def _rec_inputs():
        import jax
        import jax.numpy as jnp
        _rk = jax.random.key(seed)
        x = -0.00016672 + 0.999947 * jax.random.normal(jax.random.fold_in(_rk, 1), (64, 3, 224, 224), jnp.float32)
        return x
    x = _rec_inputs()

    def _L0_tok_setup():
        import jax, jax.numpy as jnp
        import numpy as np
        P = 16
        E = 192
        C = 3
        PD = P * P * C

        def layer_norm(x, w, b, eps=1e-05):
            mu = jnp.mean(x, axis=-1, keepdims=True)
            var = jnp.mean(jnp.square(x - mu), axis=-1, keepdims=True)
            return (x - mu) * jax.lax.rsqrt(var + eps) * w + b
        key = jax.random.key(seed)
        ks = jax.random.split(key, 4)
        x = jax.random.normal(ks[0], (64, C, 96, 96), dtype=jnp.float32)
        W = jax.random.normal(ks[1], (PD, E), dtype=jnp.float32) / np.sqrt(PD)
        b = jax.random.normal(ks[2], (E,), dtype=jnp.float32) * 0.01
        ln1_w = jnp.ones((PD,), dtype=jnp.float32)
        ln1_b = jnp.zeros((PD,), dtype=jnp.float32)
        ln2_w = jnp.ones((E,), dtype=jnp.float32)
        ln2_b = jnp.zeros((E,), dtype=jnp.float32)
        return {'x': x, 'W': W, 'b': b, 'ln1_w': ln1_w, 'ln1_b': ln1_b, 'ln2_w': ln2_w, 'ln2_b': ln2_b}
    _L0_tok_all = _L0_tok_setup()
    _L0_tok_in = {k: v for k, v in _L0_tok_all.items() if k in ('W', 'b', 'ln1_w', 'ln1_b', 'ln2_w', 'ln2_b')}
    del _L0_tok_all

    def _L0_attn_setup():
        import jax, jax.numpy as jnp
        import numpy as np
        B, S, E, H = (8, 256, 192, 12)
        SPARSITY = 0.4
        key = jax.random.key(seed)
        ks = jax.random.split(key, 5)
        return {'hidden_states': jax.random.normal(ks[0], (B, S, E), dtype=jnp.float32), 'W_qkv': jax.random.normal(ks[1], (E, 3 * E), dtype=jnp.float32) * E ** (-0.5), 'b_qkv': jax.random.normal(ks[2], (3 * E,), dtype=jnp.float32) * 0.02, 'W_proj': jax.random.normal(ks[3], (E, E), dtype=jnp.float32) * E ** (-0.5), 'b_proj': jax.random.normal(ks[4], (E,), dtype=jnp.float32) * 0.02}
    _L0_attn_all = _L0_attn_setup()
    _L0_attn_in = {k: v for k, v in _L0_attn_all.items() if k in ('W_qkv', 'b_qkv', 'W_proj', 'b_proj')}
    del _L0_attn_all

    def _L0_ffn_setup():
        import jax, jax.numpy as jnp
        import numpy as np
        TOP_K = 2

        def _moe(x, Wg, bg, W1, b1, W2, b2):
            B, S, D = x.shape
            E = Wg.shape[1]
            logits = x @ Wg + bg
            top_vals, top_idx = jax.lax.top_k(logits, TOP_K)
            gates_k = jax.nn.softmax(top_vals, axis=-1)
            one_hot = jax.nn.one_hot(top_idx, E, dtype=x.dtype)
            gates = jnp.sum(one_hot * gates_k[..., None], axis=-2)
            flat_x = x.reshape(-1, D)
            flat_g = gates.reshape(-1, E).T

            def body(acc, p):
                W1e, b1e, W2e, b2e, ge = p
                h = jax.nn.relu(flat_x @ W1e + b1e)
                acc = acc + (h @ W2e + b2e) * ge[:, None]
                return (acc, None)
            out, _ = jax.lax.scan(body, jnp.zeros_like(flat_x), (W1, b1, W2, b2, flat_g))
            return out.reshape(B, S, D)
        key = jax.random.key(seed)
        k = jax.random.split(key, 5)
        B, S, D, E, H = (8, 512, 192, 8, 768)
        init = lambda kk, shape: jax.random.normal(kk, shape, jnp.float32) * 0.02
        return {'x': jax.random.normal(k[0], (B, S, D), jnp.float32), 'Wg': init(k[1], (D, E)), 'bg': jnp.zeros((E,), jnp.float32), 'W1': init(k[2], (E, D, H)), 'b1': jnp.zeros((E, H), jnp.float32), 'W2': init(k[3], (E, H, D)), 'b2': jnp.zeros((E, D), jnp.float32)}
    _L0_ffn_all = _L0_ffn_setup()
    _L0_ffn_in = {k: v for k, v in _L0_ffn_all.items() if k in ('Wg', 'bg', 'W1', 'b1', 'W2', 'b2')}
    del _L0_ffn_all
    return {'x': x, 'L0_tok_W': _L0_tok_in['W'], 'L0_tok_b': _L0_tok_in['b'], 'L0_tok_ln1_w': _L0_tok_in['ln1_w'], 'L0_tok_ln1_b': _L0_tok_in['ln1_b'], 'L0_tok_ln2_w': _L0_tok_in['ln2_w'], 'L0_tok_ln2_b': _L0_tok_in['ln2_b'], 'L0_attn_W_qkv': _L0_attn_in['W_qkv'], 'L0_attn_b_qkv': _L0_attn_in['b_qkv'], 'L0_attn_W_proj': _L0_attn_in['W_proj'], 'L0_attn_b_proj': _L0_attn_in['b_proj'], 'L0_ffn_Wg': _L0_ffn_in['Wg'], 'L0_ffn_bg': _L0_ffn_in['bg'], 'L0_ffn_W1': _L0_ffn_in['W1'], 'L0_ffn_b1': _L0_ffn_in['b1'], 'L0_ffn_W2': _L0_ffn_in['W2'], 'L0_ffn_b2': _L0_ffn_in['b2']}

def reference(x, L0_tok_W, L0_tok_b, L0_tok_ln1_w, L0_tok_ln1_b, L0_tok_ln2_w, L0_tok_ln2_b, L0_attn_W_qkv, L0_attn_b_qkv, L0_attn_W_proj, L0_attn_b_proj, L0_ffn_Wg, L0_ffn_bg, L0_ffn_W1, L0_ffn_b1, L0_ffn_W2, L0_ffn_b2):
    import jax
    import jax.numpy as jnp

    def _L0_tok_ref(x, W, b, ln1_w, ln1_b, ln2_w, ln2_b):
        import jax, jax.numpy as jnp
        import numpy as np
        P = 16
        E = 192
        C = 3
        PD = P * P * C

        def layer_norm(x, w, b, eps=1e-05):
            mu = jnp.mean(x, axis=-1, keepdims=True)
            var = jnp.mean(jnp.square(x - mu), axis=-1, keepdims=True)
            return (x - mu) * jax.lax.rsqrt(var + eps) * w + b
        B, c, H, Wd = x.shape
        h, w = (H // P, Wd // P)
        p = x.reshape(B, c, h, P, w, P)
        p = p.transpose(0, 2, 4, 3, 5, 1)
        p = p.reshape(B, h * w, P * P * c)
        p = layer_norm(p, ln1_w, ln1_b)
        y = jnp.einsum('bnd,de->bne', p, W) + b
        return layer_norm(y, ln2_w, ln2_b)

    def _L0_attn_ref(hidden_states, W_qkv, b_qkv, W_proj, b_proj):
        import jax, jax.numpy as jnp
        import numpy as np
        B, S, E, H = (8, 256, 192, 12)
        SPARSITY = 0.4
        bsz, tgt_len, embed_dim = hidden_states.shape
        head_dim = embed_dim // H
        scale = head_dim ** (-0.5)
        qkv = (hidden_states @ W_qkv + b_qkv).reshape(bsz, tgt_len, 3, H, head_dim)
        qkv = qkv.transpose(2, 0, 3, 1, 4)
        q, k, v = (qkv[0], qkv[1], qkv[2])
        attn_weights = jnp.einsum('bhqd,bhkd->bhqk', q, k) * scale
        top_k = max(1, int(SPARSITY * tgt_len))
        top_k = min(top_k, tgt_len)
        kth = jax.lax.top_k(attn_weights, top_k)[0][..., -1:]
        min_val = jnp.finfo(attn_weights.dtype).min
        sparse_weights = jnp.where(attn_weights >= kth, attn_weights, min_val)
        attn = jax.nn.softmax(sparse_weights.astype(jnp.float32), axis=-1)
        attn = attn.astype(v.dtype)
        out = jnp.einsum('bhqk,bhkd->bqhd', attn, v).reshape(bsz, tgt_len, embed_dim)
        return out @ W_proj + b_proj

    def _L0_ffn_ref(x, Wg, bg, W1, b1, W2, b2):
        import jax, jax.numpy as jnp
        import numpy as np
        TOP_K = 2

        def _moe(x, Wg, bg, W1, b1, W2, b2):
            B, S, D = x.shape
            E = Wg.shape[1]
            logits = x @ Wg + bg
            top_vals, top_idx = jax.lax.top_k(logits, TOP_K)
            gates_k = jax.nn.softmax(top_vals, axis=-1)
            one_hot = jax.nn.one_hot(top_idx, E, dtype=x.dtype)
            gates = jnp.sum(one_hot * gates_k[..., None], axis=-2)
            flat_x = x.reshape(-1, D)
            flat_g = gates.reshape(-1, E).T

            def body(acc, p):
                W1e, b1e, W2e, b2e, ge = p
                h = jax.nn.relu(flat_x @ W1e + b1e)
                acc = acc + (h @ W2e + b2e) * ge[:, None]
                return (acc, None)
            out, _ = jax.lax.scan(body, jnp.zeros_like(flat_x), (W1, b1, W2, b2, flat_g))
            return out.reshape(B, S, D)
        return _moe(x, Wg, bg, W1, b1, W2, b2)
    h = _L0_tok_ref(x, L0_tok_W, L0_tok_b, L0_tok_ln1_w, L0_tok_ln1_b, L0_tok_ln2_w, L0_tok_ln2_b)
    h = _layernorm(h + _L0_attn_ref(h, L0_attn_W_qkv, L0_attn_b_qkv, L0_attn_W_proj, L0_attn_b_proj), axis=-1)
    h = _layernorm(h + _L0_ffn_ref(h, L0_ffn_Wg, L0_ffn_bg, L0_ffn_W1, L0_ffn_b1, L0_ffn_W2, L0_ffn_b2), axis=-1)
    return h

_drawn_inputs = setup_inputs


def setup_inputs(seed=0):
    import zlib

    import numpy as np

    out = dict(_drawn_inputs(seed))
    spreads = {'L0_tok_ln1_w': (1.0, 0.2),
     'L0_tok_ln1_b': (0.0, 0.1),
     'L0_tok_ln2_w': (1.0, 0.2),
     'L0_tok_ln2_b': (0.0, 0.1),
     'L0_ffn_bg': (0.0, 0.1),
     'L0_ffn_b1': (0.0, 0.299),
     'L0_ffn_b2': (0.0, 0.1)}
    factors = {'L0_tok_b': 3.285, 'L0_attn_b_proj': 2.704}
    for name, (base, spread) in spreads.items():
        noise = np.random.default_rng([zlib.crc32(name.encode()), seed]).standard_normal(out[name].shape)
        drawn = base * np.exp(spread * noise) if base else spread * noise
        out[name] = jnp.asarray(drawn.astype(out[name].dtype))
    for name, factor in factors.items():
        out[name] = (out[name] * factor).astype(out[name].dtype)
    return out
```

```python
from contextlib import ExitStack

import concourse.bass as bass
from concourse import mybir

F32 = mybir.dt.float32
I32 = mybir.dt.int32
U32 = mybir.dt.uint32
ALU = mybir.AluOpType
ACT = mybir.ActivationFunctionType

EPS = 1e-5
PATCH, CH, SIDE = 16, 3, 14
EMB, HEADS, DH = 192, 12, 16
TOK = SIDE * SIDE
BT = TOK // 2
NB = 4
PT_ = NB * BT
PD = PATCH * PATCH * CH
NC = PD // 128
KB = EMB - 128 + 1
GH = 8
GROUPS = 3
ROWS = GH * TOK
TILES = 13
TR = -(-ROWS // TILES)
SLOTS = 7
PS = GROUPS * SLOTS
KEEP = int(0.4 * TOK)
NEG = -3.0e38
EX, HID = 8, 768
HC = HID // 128
UNITS = EX * HC
SCALE = DH ** -0.5
LEAD = 3


def tiles_of(j):
    return [t for t in (2 * j, 2 * j + 1) if t < TILES]


def rows_of(t):
    return min(TR, ROWS - t * TR)


def units_of(g, j):
    s = 7 * (g - 1) + j if g else 14 + j
    if g == 0 and j > 2:
        return []
    return list(range(3 * s, min(3 * s + 3, UNITS))) if s < 14 else list(range(42 + 2 * (s - 14), 44 + 2 * (s - 14)))


class Count:

    def __init__(self):
        self.n, self.off = 0, 0

    def add(self):
        self.n += 1
        return self.n + self.off

    def now(self):
        return self.n + self.off


def vit_kernel(nc, x, tok_W, tok_b, ln1_w, ln1_b, ln2_w, ln2_b, W_qkv, b_qkv, W_proj, b_proj,
               Wg, bg, W1, b1, W2, b2, out):
    NIMG = x.shape[0]
    PAIRS = NIMG // 2
    LOOP0, LOOP1 = 3, PAIRS - 1

    with ExitStack() as ctx:
        def sb(name, shape, dt=F32):
            return ctx.enter_context(nc.sbuf_tensor(name, shape, dt))

        def pb(name, shape):
            return ctx.enter_context(nc.psum_tensor(name, shape, F32))

        def sem(name):
            return ctx.enter_context(nc.semaphore(name))

        w_tok = sb("w_tok", [128, NC, EMB])
        lnw_col = sb("lnw_col", [128, NC])
        lnb_col = sb("lnb_col", [128, NC])
        cv = sb("cv", [BT, EMB])
        ln2w_bc = sb("ln2w_bc", [BT, EMB])
        ln2b_bc = sb("ln2b_bc", [BT, EMB])
        bproj_bc = sb("bproj_bc", [BT, EMB])
        wqkvA = sb("wqkvA", [128, 3 * EMB])
        wqkvB = sb("wqkvB", [KB, 3 * EMB])
        wcA = sb("wcA", [128, 2, 192])
        wcB = sb("wcB", [KB, 2, 192])
        wpA = sb("wpA", [128, EMB])
        wpC = sb("wpC", [128, EMB])
        wgA = sb("wgA", [128, EX])
        wgB = sb("wgB", [KB, EX])
        w1A = sb("w1A", [128, EX, HID])
        w1B = sb("w1B", [KB, EX, HID])
        w2 = sb("w2", [128, UNITS, EMB])
        b2s = sb("b2s", [EX, EMB])
        ident = sb("ident", [128, 128])
        hmask = sb("hmask", [128, GH])
        sel = sb("sel", [EX, EX, 128])
        ones_row = sb("ones_row", [1, BT])
        mhalf = sb("mhalf", [BT, NB])
        io_i = sb("io_i", [BT, EX], I32)
        io_f = sb("io_f", [BT, EX])
        xt = sb("xt", [BT, NB, PD])
        xT = sb("xT", [128, NC, TOK])
        st1 = sb("st1", [BT, NB, 2, 6])
        mv1 = sb("mv1", [BT, NB, 2])
        rs1 = sb("rs1", [BT, NB])
        nm1 = sb("nm1", [BT, NB])
        st2 = sb("st2", [BT, NB, 6])
        mv2 = sb("mv2", [BT, NB, 2])
        rs2 = sb("rs2", [BT, NB])
        nm2 = sb("nm2", [BT, NB])
        h0 = sb("h0", [BT, NB, EMB])
        hb = sb("hb", [BT, NB, EMB])
        h0tA = sb("h0tA", [128, PT_])
        h0tB = sb("h0tB", [KB, PT_])
        qk = sb("qk", [128, 2, TOK])
        qm = sb("qm", [128, GH, TOK])
        vz = sb("vz", [BT, 2, GH * 144])
        S = sb("S", [TR, TILES, TOK])
        E = sb("E", [TR, 3, 2, TOK])
        work = sb("work", [TR, 2, TOK])
        m8 = sb("m8", [TR, 2, 2, 8])
        top8 = sb("top8", [TR, TILES, 8])
        kth8 = sb("kth8", [TR, TILES, 8])
        nb = sb("nb", [TR, TILES])
        rsum = sb("rsum", [TR, TILES])
        rinv = sb("rinv", [TR, TILES])
        Pt = sb("Pt", [BT, 2, TILES * TR])
        ot = sb("ot", [128, GROUPS, TOK])
        att = sb("att", [BT, NB, EMB])
        tokb_row, cv_row = att[0:1, 0, :], att[0:1, 1, :]
        stA = sb("stA", [BT, NB, 6])
        mvA = sb("mvA", [BT, NB, 2])
        rsA = sb("rsA", [BT, NB])
        nmA = sb("nmA", [BT, NB])
        h1 = sb("h1", [BT, NB, EMB])
        h1tA = sb("h1tA", [128, PT_])
        h1tB = sb("h1tB", [KB, PT_])
        lg = sb("lg", [BT, NB, EX])
        lg8 = sb("lg8", [BT, NB, 8])
        ix8 = sb("ix8", [BT, NB, 8], U32)
        ixf = sb("ixf", [BT, NB, 8])
        dm = sb("dm", [BT, NB])
        e2 = sb("e2", [BT, NB])
        g12 = sb("g12", [BT, NB, 3])
        oh = sb("oh", [BT, 2, NB, EX])
        gates = sb("gates", [BT, NB, EX])
        gT = sb("gT", [EX, PT_])
        G = sb("G", [128, PT_])
        xgA = sb("xgA", [128, 2, PT_])
        xgB = sb("xgB", [KB, 2, PT_])
        hs = sb("hs", [128, 2, PT_])
        ysb = sb("ysb", [BT, NB, EMB])
        stB = sb("stB", [BT, NB, 6])
        mvB = sb("mvB", [BT, NB, 2])
        rsB = sb("rsB", [BT, NB])
        nmB = sb("nmB", [BT, NB])

        psS = [pb(f"psS{i}", [128, 2, TOK]) for i in range(2)]
        psT = pb("psT", [128, 2, 2, TR])
        psM = pb("psM", [128, 512])
        psH = [pb(f"psH{i}", [128, PT_]) for i in range(2)]
        psY = [pb(f"psY{i}", [128, 2, EMB]) for i in range(2)]

        w_in, pool_c, dve_c, act_c = sem("w_in"), sem("pool_c"), sem("dve_c"), sem("act_c")
        const_ok, wtok_ok, cvrow_ok, cv_ok = sem("const_ok"), sem("wtok_ok"), sem("cvrow_ok"), sem("cv_ok")
        passed = sem("passed")
        x_in = sem("x_in")
        ln1_stats, ln1_rstd, xn_ok = sem("ln1_stats"), sem("ln1_rstd"), sem("xn_ok")
        ma_full, ma_free = sem("ma_full"), sem("ma_free")
        y_evac, yb_ok, ln2_stats, h0_ok = sem("y_evac"), sem("yb_ok"), sem("ln2_stats"), sem("h0_ok")
        h0t_ok, qk_ok, qm_ok, vz_ok = sem("h0t_ok"), sem("qk_ok"), sem("qm_ok"), sem("vz_ok")
        s_full, s_evac, nb_ok, e_ok = sem("s_full"), sem("s_evac"), sem("nb_ok"), sem("e_ok")
        mask_ok, p_ok, pt_full, pt_evac = sem("mask_ok"), sem("p_ok"), sem("pt_full"), sem("pt_evac")
        ot_ok, att_ok, r1_ok, lnA_stats, h1_ok = sem("ot_ok"), sem("att_ok"), sem("r1_ok"), sem("lnA_stats"), sem("h1_ok")
        h1t_ok, lg_ok, dm_ok, e2_ok, gates_ok, gT_ok = (sem("h1t_ok"), sem("lg_ok"), sem("dm_ok"), sem("e2_ok"),
                                                        sem("gates_ok"), sem("gT_ok"))
        G_ok, xg_ok, h_full, h_evac, l2_done, y2_evac = (sem("G_ok"), sem("xg_ok"), sem("h_full"), sem("h_evac"),
                                                         sem("l2_done"), sem("y2_evac"))
        r2_ok, lnB_stats, out_ok, out_dma = sem("r2_ok"), sem("lnB_stats"), sem("out_ok"), sem("out_dma")

        def n_of(k, g, j):
            return PS * k + SLOTS * g + j

        def has(kk, g, j, d=0):
            return 0 <= PS * kk + SLOTS * g + j + d < PS * PAIRS

        def pair_ok(kk):
            return 0 <= kk < PAIRS

        def schedule(eng, slot, chain=None, chain_sem=None, counts=(), latest=None):
            def iteration(k, kk):
                for g in range(GROUPS):
                    for j in range(SLOTS):
                        slot(k, kk, g, j)
                if chain and chain.n:
                    eng.wait_ge(chain_sem, chain.n)
                    eng.sem_clear(chain_sem)
                    chain.n = 0

            for k in range(LOOP0):
                iteration(k, k)
            before = [c.n for c, _ in counts]
            with eng.Fori(LOOP0, LOOP1) as k:
                for c, per in counts:
                    c.off = (k - LOOP0) * per
                if latest:
                    (s, v), = latest
                    latest[:] = [(s, v + (k - LOOP0) * EX)]
                iteration(k, LOOP0)
            for (c, per), n in zip(counts, before):
                assert c.n - n == per, (c.n - n, per)
                c.off = 0
                c.n = n + per * (LOOP1 - LOOP0)
            if latest:
                latest[:] = [(s, v + (LOOP1 - LOOP0) * EX)]
            for k in range(LOOP1, PAIRS + 2):
                iteration(k, k)

        block = ctx.enter_context(nc.Block())

        @block.sync
        def _(sp):
            def load(k):
                for im in range(2):
                    for hf in range(2):
                        for c in range(CH):
                            src = x[bass.ds(2 * k + im, 1), c, hf * 112:hf * 112 + 112, :]
                            sp.dma_start(
                                xt[:, 2 * im + hf, c * 256:(c + 1) * 256].rearrange("p (i j) -> p i j", j=PATCH),
                                src.rearrange("o (h i) (w j) -> w (o h) i j", i=PATCH, j=PATCH)).then_inc(x_in, 16)

            def store(k):
                sp.wait_ge(out_ok, k + 1)
                for im in range(2):
                    for hf in range(2):
                        dst = out[bass.ds(2 * k + im, 1), hf * BT:(hf + 1) * BT, :]
                        sp.dma_start(dst.rearrange("o (h w) e -> w (o h) e", w=SIDE), ysb[:, 2 * im + hf, :]) \
                          .then_inc(out_dma, 16)

            load(0)
            sp.wait_ge(y_evac, 2)
            load(1)
            for k in range(2):
                sp.wait_ge(y_evac, 2 * k + 4)
                load(k + 2)
            with sp.Fori(2, PAIRS - 2) as k:
                sp.wait_ge(y_evac, 2 * k + 4)
                load(k + 2)
                store(k - 2)
            for k in range(PAIRS - 4, PAIRS):
                store(k)
            sp.wait_ge(out_dma, 64 * PAIRS)

        @block.gpsimd
        def _(pool):
            chain = Count()

            def link(ins):
                ins.then_inc(pool_c, 1)
                pool.wait_ge(pool_c, chain.add())

            link(pool.memset(ident[:], 0.0))
            link(pool.affine_select(out=ident[:], in_=ident[:], compare_op=ALU.not_equal, fill=1.0, base=0,
                                    pattern=[[-1, 128]], channel_multiplier=1))
            link(pool.memset(hmask[:], 1.0))
            link(pool.affine_select(out=hmask[:], in_=hmask[:], compare_op=ALU.is_ge, fill=0.0, base=0,
                                    pattern=[[-DH, GH]], channel_multiplier=1))
            link(pool.affine_select(out=hmask[:], in_=hmask[:], compare_op=ALU.is_ge, fill=0.0, base=DH - 1,
                                    pattern=[[DH, GH]], channel_multiplier=-1))
            link(pool.memset(sel[:], 0.0))
            link(pool.affine_select(out=sel[:], in_=sel[:], compare_op=ALU.not_equal, fill=1.0, base=0,
                                    pattern=[[-1, EX], [0, 128]], channel_multiplier=1))
            link(pool.iota(io_i[:], [[1, EX]], base=0, channel_multiplier=0))
            link(pool.tensor_copy(io_f[:], io_i[:]))
            link(pool.memset(ones_row[:], 1.0))
            link(pool.memset(mhalf[:], -0.5))
            link(pool.memset(vz[:], 0.0))
            link(pool.memset(h0tB[64:65, :], 1.0))
            link(pool.memset(h1tB[64:65, :], 1.0))
            link(pool.memset(wcA[:], 0.0))
            link(pool.memset(wcB[:], 0.0))
            loads = []
            for hf in range(2):
                part, cols = slice(hf * 384, hf * 384 + 384), slice(CH * hf, CH * hf + CH)
                loads += [(w_tok[:, cols, :], tok_W[part].rearrange("(p c) e -> p c e", c=CH)),
                          (lnw_col[:, cols], ln1_w[part].rearrange("(p c) -> p c", c=CH)),
                          (lnb_col[:, cols], ln1_b[part].rearrange("(p c) -> p c", c=CH))]

            def row(v):
                return v.rearrange("(a n) -> a n", a=1)

            loads += [(tokb_row, row(tok_b))]
            loads += [(t[:], row(v).broadcast_to([BT, EMB])) for t, v in
                      ((ln2w_bc, ln2_w), (ln2b_bc, ln2_b), (bproj_bc, b_proj))]
            loads += [(wqkvA[:], W_qkv[0:128]), (wqkvB[0:64], W_qkv[128:192]), (wqkvB[64:65], row(b_qkv))]
            for i in range(2):
                cols = slice(i * EMB + 128, i * EMB + 192)
                loads += [(wcA[:, i, 64:128], W_qkv[0:128, cols]), (wcB[0:64, i, 64:128], W_qkv[128:192, cols]),
                          (wcB[64:65, i, 64:128], row(b_qkv)[:, cols])]
            loads += [(wpA[:], W_proj[0:128]), (wpC[0:64], W_proj[128:192]), (wpC[64:128], W_proj[128:192])]
            loads += [(wgA[:], Wg[0:128]), (wgB[0:64], Wg[128:192]), (wgB[64:65], row(bg))]
            loads += [(w1A[:], W1[:, 0:128, :].rearrange("e p n -> p e n")),
                      (w1B[0:64], W1[:, 128:192, :].rearrange("e p n -> p e n")),
                      (w1B[64:65], b1.rearrange("(a e) n -> a e n", a=1)),
                      (w2[:], W2.rearrange("e (c p) n -> p (e c) n", p=128)), (b2s[:], b2)]
            assert len(loads) == NLOADS, len(loads)
            for dst, src in loads:
                pool.dma_start(dst, src).then_inc(w_in, 16)
            pool.memset(nm1[:], 0.0).then_inc(const_ok, 1)

            def rstd_of(mv, rs, nm):
                link(pool.tensor_scalar(rs[:], mv[:, :, 1], EPS, None, ALU.add))
                link(pool.tensor_tensor(rs[:], rs[:], mhalf[:], ALU.pow))
                link(pool.tensor_tensor(nm[:], mv[:, :, 0], rs[:], ALU.mult))
                ins = pool.tensor_scalar(nm[:], nm[:], -1.0, 1.0, ALU.mult, ALU.mult)
                return ins

            def normalise(dst, src, rs, nm):
                for b in range(NB):
                    ins = pool.tensor_scalar(dst[:, b, :], src[:, b, :], rs[:, b:b + 1], nm[:, b:b + 1], ALU.mult, ALU.add)
                return ins

            def ln1(k):
                pool.wait_ge(ln1_stats, k + 1)
                pool.sem_inc(passed, 1)
                rstd_of(mv1, rs1, nm1).then_inc(ln1_rstd, 1)

            def bc(t):
                return t[:, :].unsqueeze(1).broadcast_to([BT, NB, EMB])

            def y_bias(k):
                pool.wait_ge(y_evac, 2 * k + 2)
                pool.tensor_tensor(h0[:], h0[:], bc(cv), ALU.add).then_inc(yb_ok, 1)

            def ln2(k):
                pool.wait_ge(ln2_stats, k + 1)
                pool.sem_inc(passed, 1)
                link(rstd_of(mv2, rs2, nm2))
                link(normalise(h0, h0, rs2, nm2))
                link(pool.tensor_tensor(h0[:], h0[:], bc(ln2w_bc), ALU.mult))
                pool.tensor_tensor(h0[:], h0[:], bc(ln2b_bc), ALU.add).then_inc(h0_ok, 1)

            def q_masked(k, g):
                pool.wait_ge(qk_ok, GROUPS * k + g + 1)
                pool.tensor_tensor(qm[:], qk[:, 0, :].unsqueeze(1).broadcast_to([128, GH, TOK]),
                                   hmask[:, :].unsqueeze(2).broadcast_to([128, GH, TOK]), ALU.mult).then_inc(qm_ok, 1)

            def norm_p(k, g, j, d):
                pool.wait_ge(mask_ok, n_of(k, g, j) + d + 1)
                pool.sem_inc(passed, 1)
                for i, t in enumerate(tiles_of((j + d) % SLOTS)):
                    R, e = rows_of(t), (SLOTS * g + j + d) % 3
                    ins = pool.tensor_scalar(E[0:R, e, i, :], E[0:R, e, i, :], rinv[0:R, t:t + 1], 1.0, ALU.mult, ALU.mult)
                ins.then_inc(p_ok, 1)

            def x_gated(k, e):
                pool.wait_ge(G_ok, EX * k + e + 1)
                need = UNITS * k + HC * (e - 1)
                if not isinstance(need, int) or need > 0:
                    pool.wait_ge(h_full, need)
                pool.tensor_tensor(xgA[:, e % 2, :], h1tA[:], G[:], ALU.mult)
                pool.tensor_tensor(xgB[:, e % 2, :], h1tB[:], G[0:KB, :], ALU.mult).then_inc(xg_ok, 1)

            pool.wait_ge(w_in, 16 * NLOADS)
            ln1(0)
            pool.wait_ge(cv_ok, 1)
            y_bias(0)
            ln2(0)
            q_masked(0, 0)

            def slot(k, kk, g, j):
                if g == 0 and j == 3 and pair_ok(kk - 2):
                    pool.wait_ge(y2_evac, 2 * (k - 2) + 2)
                    pool.tensor_tensor(ysb[:], ysb[:], h1[:], ALU.add).then_inc(r2_ok, 1)
                if g == 0 and j == 3 and pair_ok(kk - 1):
                    pool.wait_ge(att_ok, 2 * (k - 1) + 2)
                    pool.tensor_tensor(att[:], att[:], hb[:], ALU.add).then_inc(r1_ok, 1)
                if g == 0 and j == 4:
                    if pair_ok(kk - 1):
                        pool.wait_ge(lnA_stats, k)
                        pool.sem_inc(passed, 1)
                        link(rstd_of(mvA, rsA, nmA))
                        if pair_ok(kk - 2):
                            pool.wait_ge(r2_ok, k - 1)
                        normalise(h1, att, rsA, nmA).then_inc(h1_ok, 1)
                        pool.wait_ge(r1_ok, k)
                    if pair_ok(kk):
                        pool.wait_ge(h0_ok, k + 1)
                        link(pool.tensor_tensor(hb[:], h0[:], bc(bproj_bc), ALU.add))
                if g == 0 and j == 5 and pair_ok(kk - 2):
                    pool.wait_ge(lnB_stats, k - 1)
                    pool.sem_inc(passed, 1)
                    link(rstd_of(mvB, rsB, nmB))
                    normalise(ysb, ysb, rsB, nmB).then_inc(out_ok, 1)
                if g == 1 and j == 5 and pair_ok(kk + 1):
                    ln1(k + 1)
                if g == 2 and j == 1 and pair_ok(kk + 1):
                    y_bias(k + 1)
                if g == 2 and j == 2 and pair_ok(kk + 1):
                    ln2(k + 1)
                if j == 3 and has(kk, g, j, 4):
                    q_masked(k if g < 2 else k + 1, (g + 1) % GROUPS)
                if g == 1 and j == 0 and pair_ok(kk - 1):
                    x_gated(k - 1, 0)
                kp = 2 if g == 0 else 1
                if pair_ok(kk - kp):
                    for u in units_of(g, j):
                        if u % HC == 2 and u // HC + 1 < EX:
                            x_gated(k - kp, u // HC + 1)
                if has(kk, g, j, -1):
                    norm_p(k, g, j, -1)

            schedule(pool, slot, chain, pool_c)

        @block.vector
        def _(dve):
            chain = Count()

            def tick(ins):
                ins.then_inc(dve_c, 1)
                return chain.add()

            def need(v):
                dve.wait_ge(dve_c, v)

            dve.wait_ge(w_in, 16 * NLOADS)
            dve.wait_ge(cvrow_ok, 1)
            for c in range(NC):
                ins = dve.tensor_scalar(w_tok[:, c, :], w_tok[:, c, :], lnw_col[:, c:c + 1], None, ALU.mult)
            ins.then_inc(wtok_ok, 1)
            dve.wait_ge(const_ok, 1)

            def ln1(k):
                dve.wait_ge(x_in, 192 * (k + 1))
                for b in range(NB):
                    for c in range(2):
                        v = tick(dve.bn_stats(st1[:, b, c, :], xt[:, b, c * 384:(c + 1) * 384]))
                need(v)
                for b in range(NB):
                    ins = dve.bn_aggr(mv1[:, b, :], st1[:, b, :, :])
                ins.then_inc(ln1_stats, 1)

            def ln(src, st, mv, done):
                for b in range(NB):
                    v = tick(dve.bn_stats(st[:, b, :], src[:, b, :]))
                need(v)
                for b in range(NB):
                    ins = dve.bn_aggr(mv[:, b, :], st[:, b, :])
                ins.then_inc(done, 1)

            def select(k, g, j):
                dve.wait_ge(s_evac, n_of(k, g, j) + 1)
                dve.sem_inc(passed, 1)
                ts = tiles_of(j)
                R = rows_of(ts[0])
                at = {}
                rounds = -(-KEEP // 8)
                for r in range(rounds):
                    for i, t in enumerate(ts):
                        src = S[0:R, t, :] if r == 0 else work[0:R, i, :]
                        dst = top8[0:R, t, :] if r == 0 else kth8[0:R, t, :] if r == rounds - 1 else m8[0:R, i, 0, :]
                        if r:
                            need(at[i])
                        at[i] = tick(dve.max(dst, src))
                    if r < rounds - 1:
                        for i, t in enumerate(ts):
                            src = S[0:R, t, :] if r == 0 else work[0:R, i, :]
                            val = top8[0:R, t, :] if r == 0 else m8[0:R, i, 0, :]
                            need(at[i])
                            at[i] = tick(dve.match_replace(work[0:R, i, :], val, src, NEG))
                need(at[len(ts) - 1])
                dve.tensor_scalar(nb[0:R, 2 * j:2 * j + len(ts)], top8[0:R, 2 * j:2 * j + len(ts), 0], -SCALE, None,
                                  ALU.mult).then_inc(nb_ok, 1)

            def mask(k, g, j, d):
                dve.wait_ge(e_ok, n_of(k, g, j) + d + 1)
                ts = tiles_of((j + d) % SLOTS)
                R = rows_of(ts[0])
                e = (SLOTS * g + j + d) % 3
                for i, t in enumerate(ts):
                    v = tick(dve.scalar_tensor_tensor(out=E[0:R, e, i, :], in0=S[0:R, t, :],
                                                      scalar=kth8[0:R, t, (KEEP - 1) % 8:(KEEP - 1) % 8 + 1],
                                                      in1=E[0:R, e, i, :], op0=ALU.is_ge, op1=ALU.mult,
                                                      accum_out=rsum[0:R, t:t + 1]))
                need(v)
                dve.reciprocal(rinv[0:R, ts[0]:ts[-1] + 1], rsum[0:R, ts[0]:ts[-1] + 1]).then_inc(mask_ok, 1)

            def gate_top(k):
                dve.wait_ge(lg_ok, k + 1)
                dve.sem_inc(passed, 1)
                for b in range(NB):
                    v = tick(dve.max(lg8[:, b, :], lg[:, b, :]))
                need(v)
                for b in range(NB):
                    v = tick(dve.max_index(ix8[:, b, :], lg8[:, b, :], lg[:, b, :]))
                dve.tensor_tensor(dm[:], lg8[:, :, 1], lg8[:, :, 0], ALU.subtract).then_inc(dm_ok, 1)
                need(v)
                tick(dve.tensor_copy(ixf[:], ix8[:]))

            def gate_mix(k):
                dve.wait_ge(e2_ok, k + 1)
                need(tick(dve.tensor_scalar(g12[:, :, 2], e2[:], 1.0, None, ALU.add)))
                need(tick(dve.reciprocal(g12[:, :, 0], g12[:, :, 2])))
                need(tick(dve.tensor_tensor(g12[:, :, 1], g12[:, :, 0], e2[:], ALU.mult)))
                io = io_f[:, :].unsqueeze(1).broadcast_to([BT, NB, EX])
                for i in range(2):
                    v = tick(dve.tensor_tensor(oh[:, i], io, ixf[:, :, i:i + 1].broadcast_to([BT, NB, EX]), ALU.is_equal))
                need(v)
                for i in range(2):
                    v = tick(dve.tensor_tensor(oh[:, i], oh[:, i], g12[:, :, i:i + 1].broadcast_to([BT, NB, EX]), ALU.mult))
                need(v)
                dve.tensor_tensor(gates[:], oh[:, 0], oh[:, 1], ALU.add).then_inc(gates_ok, 1)

            ln1(0)
            dve.wait_ge(yb_ok, 1)
            ln(h0, st2, mv2, ln2_stats)

            def slot(k, kk, g, j):
                if has(kk, g, j):
                    select(k, g, j)
                if has(kk, g, j, -1):
                    mask(k, g, j, -1)
                if g == 0 and j == 3 and pair_ok(kk - 1):
                    dve.wait_ge(r1_ok, k)
                    ln(att, stA, mvA, lnA_stats)
                if g == 0 and j == 4 and pair_ok(kk - 2):
                    dve.wait_ge(r2_ok, k - 1)
                    ln(ysb, stB, mvB, lnB_stats)
                if g == 0 and j == 5 and pair_ok(kk - 1):
                    gate_top(k - 1)
                if g == 0 and j == 6 and pair_ok(kk - 1):
                    gate_mix(k - 1)
                if g == 1 and j == 4 and pair_ok(kk + 1):
                    ln1(k + 1)
                if g == 2 and j == 1 and pair_ok(kk + 1):
                    dve.wait_ge(yb_ok, k + 2)
                    ln(h0, st2, mv2, ln2_stats)

            schedule(dve, slot, chain, dve_c)

        @block.scalar
        def _(act):
            ma = Count()

            def ma_take():
                act.wait_ge(ma_full, ma.add())

            def tok1(k):
                act.wait_ge(ln1_rstd, k + 1)
                for b in range(NB):
                    ins = act.activation(xt[:, b, :], xt[:, b, :], ACT.Identity, bias=nm1[:, b:b + 1], scale=rs1[:, b:b + 1])
                ins.then_inc(xn_ok, 1)
                for i in range(2):
                    for c in range(0, NC, 2):
                        ma_take()
                        act.activation(xT[:, c:c + 2, :], psM[:, 0:2 * TOK].rearrange("p (c n) -> p c n", c=2),
                                       ACT.Copy).then_inc(ma_free, 1)
                    ma_take()
                    act.activation(h0[:, 2 * i:2 * i + 2, :], psM[0:BT, 0:2 * EMB].rearrange("p (b e) -> p b e", e=EMB),
                                   ACT.Copy).then_inc(y_evac, 1)

            def transposed(A, B, done):
                ma_take()
                act.activation(A[:], psM[:, 0:PT_], ACT.Copy).then_inc(done, 1)
                ma_take()
                act.activation(B[0:64, :], psM[0:64, 0:PT_], ACT.Copy).then_inc(done, 1)

            def prep(k, g):
                ma_take()
                act.activation(qk[:], psM[:, 0:2 * TOK].rearrange("p (a n) -> p a n", a=2), ACT.Copy).then_inc(qk_ok, 1)

            def values():
                ma_take()
                for hf in range(2):
                    ins = act.activation(vz[:, hf, :].rearrange("p (h x) -> p h x", x=144)[:, :, 0:DH],
                                         psM[0:BT, hf * 128:(hf + 1) * 128].rearrange("p (h d) -> p h d", d=DH), ACT.Copy)
                ins.then_inc(vz_ok, 1)

            def s_copy(k, g, j, d):
                act.wait_ge(s_full, n_of(k, g, j) + d + 1)
                jj = (j + d) % SLOTS
                v = n_of(k, g, j) + d + 1 - SLOTS
                if not isinstance(v, int) or v > 0:
                    act.wait_ge(mask_ok, v)
                ts = tiles_of(jj)
                R = rows_of(ts[0])
                act.activation(S[0:R, ts[0]:ts[-1] + 1, :], psS[jj % 2][0:R, 0:len(ts), :], ACT.Copy).then_inc(s_evac, 1)

            def exps(k, g, j, d):
                act.wait_ge(nb_ok, n_of(k, g, j) + d + 1)
                v = n_of(k, g, j) + d + 1 - 3
                if not isinstance(v, int) or v > 0:
                    act.wait_ge(pt_full, v)
                for i, t in enumerate(tiles_of((j + d) % SLOTS)):
                    R, e = rows_of(t), (SLOTS * g + j + d) % 3
                    ins = act.activation(E[0:R, e, i, :], S[0:R, t, :], ACT.Exp, bias=nb[0:R, t:t + 1], scale=SCALE)
                ins.then_inc(e_ok, 1)

            def pt_copy(k, g, j, d):
                act.wait_ge(pt_full, n_of(k, g, j) + d + 1)
                ts = tiles_of((j + d) % SLOTS)
                R = rows_of(ts[0])
                dst = Pt[:, :, ts[0] * TR:(ts[-1] + 1) * TR].rearrange("p f (t r) -> p t f r", r=TR)[:, :, :, 0:R]
                act.activation(dst, psT[0:BT, 0:len(ts), :, 0:R], ACT.Copy).then_inc(pt_evac, 1)

            def g_copy(k, e):
                v = EX * k + e
                if not isinstance(v, int) or v > 0:
                    act.wait_ge(xg_ok, v)
                ma_take()
                act.activation(G[:], psM[:, 0:PT_], ACT.Copy).then_inc(G_ok, 1)

            def relu(k, u):
                v = UNITS * k + u
                act.wait_ge(h_full, v + 1)
                if not isinstance(v, int) or v > 1:
                    act.wait_ge(l2_done, v - 1)
                act.activation(hs[:, u % 2, :], psH[u % 2][:], ACT.Relu).then_inc(h_evac, 1)

            ma_take()
            act.activation(cv_row, psM[0:1, 0:EMB], ACT.Copy).then_inc(cvrow_ok, 1)
            ma_take()
            act.activation(cv[:], psM[0:BT, 0:EMB], ACT.Copy).then_inc(cv_ok, 1)
            tok1(0)
            act.wait_ge(const_ok, 1)
            transposed(h0tA, h0tB, h0t_ok)
            prep(0, 0)
            for j in range(LEAD):
                s_copy(0, 0, j, 0)

            def slot(k, kk, g, j):
                if has(kk, g, j, -1):
                    exps(k, g, j, -1)
                if g == 2 and j == 0 and pair_ok(kk + 1):
                    tok1(k + 1)
                if j == 2 and has(kk, g, j, -SLOTS):
                    ma_take()
                    act.activation(ot[:, (g - 1) % GROUPS, :], psM[:, 0:TOK], ACT.Copy).then_inc(ot_ok, 1)
                if has(kk, g, j, -2):
                    pt_copy(k, g, j, -2)
                if has(kk, g, j, LEAD):
                    s_copy(k, g, j, LEAD)
                if j == 2 and has(kk, g, j, -SLOTS):
                    if g == 0:
                        if kk - 1 > 0:
                            act.wait_ge(lnA_stats, k - 1)
                            act.wait_ge(h1_ok, k - 1)
                        for i in range(2):
                            ma_take()
                            act.activation(att[:, 2 * i:2 * i + 2, :],
                                           psM[0:BT, 0:2 * EMB].rearrange("p (b e) -> p b e", e=EMB),
                                           ACT.Copy).then_inc(att_ok, 1)
                if j == 3 and has(kk, g, j):
                    values()
                    if g == 2 and pair_ok(kk + 1):
                        transposed(h0tA, h0tB, h0t_ok)
                    if has(kk, g, j, 4):
                        prep(k, g)
                if g == 0 and j == 5 and pair_ok(kk - 1):
                    transposed(h1tA, h1tB, h1t_ok)
                    ma_take()
                    act.activation(lg[:], psM[0:BT, 0:NB * EX].rearrange("p (b e) -> p b e", e=EX),
                                   ACT.Copy).then_inc(lg_ok, 1)
                if g == 0 and j == 6 and pair_ok(kk - 1):
                    act.wait_ge(dm_ok, k)
                    act.activation(e2[:], dm[:], ACT.Exp).then_inc(e2_ok, 1)
                if g == 1 and j == 0 and pair_ok(kk - 1):
                    ma_take()
                    act.activation(gT[:], psM[0:EX, 0:PT_], ACT.Copy).then_inc(gT_ok, 1)
                    g_copy(k - 1, 0)
                kp = 2 if g == 0 else 1
                if pair_ok(kk - kp):
                    for u in units_of(g, j):
                        relu(k - kp, u)
                        if u % HC == 2 and u // HC + 1 < EX:
                            g_copy(k - kp, u // HC + 1)
                    if g == 0 and j == 2:
                        act.wait_ge(l2_done, UNITS * (k - 1))
                        if kk - 2 > 0:
                            act.wait_ge(out_dma, 64 * (k - 2))
                        for i in range(2):
                            act.activation(ysb[:, 2 * i:2 * i + 2, :], psY[i][0:BT], ACT.Copy).then_inc(y2_evac, 1)

            schedule(act, slot, counts=[(ma, NMA)])

        @block.tensor
        def _(pe):
            last_take = []

            def ma_wait():
                for s, v in last_take:
                    pe.wait_ge(s, v)

            def ma_done(ins, s, v):
                ins.then_inc(ma_full, 1)
                last_take[:] = [(s, v)]

            free = Count()

            def tok1(k):
                pe.wait_ge(xn_ok, k + 1)
                for i in range(2):
                    for c in range(0, NC, 2):
                        ma_wait()
                        for q in range(2):
                            for b in range(2):
                                at = q * TOK + b * BT
                                ins = pe.transpose(psM[:, at:at + BT], xt[:, 2 * i + b, (c + q) * 128:(c + q + 1) * 128],
                                                   ident[0:BT, 0:BT])
                        ma_done(ins, ma_free, free.add())
                    ma_wait()
                    for b in range(2):
                        for c in range(NC):
                            ins = pe.matmul(psM[0:BT, b * EMB:(b + 1) * EMB], xT[:, c, b * BT:(b + 1) * BT],
                                            w_tok[:, CH * (c % 2) + c // 2, :], start=(c == 0), stop=(c == NC - 1))
                    ma_done(ins, y_evac, 2 * k + i + 1)

            def transposes(src, k, done):
                for part, w in ((0, 128), (1, 64)):
                    ma_wait()
                    pe.sem_inc(passed, 1)
                    for b in range(NB):
                        ins = pe.transpose(psM[0:w, b * BT:(b + 1) * BT], src[:, b, part * 128:part * 128 + w],
                                           ident[0:BT, 0:BT])
                    ma_done(ins, done, 2 * k + part + 1)

            def prep(k, g):
                pe.wait_ge(h0t_ok, 2 * k + 2)
                ma_wait()
                for i in range(2):
                    dst = psM[:, i * TOK:(i + 1) * TOK]
                    if g < 2:
                        tok = slice(g * TOK, (g + 1) * TOK)
                        col = slice(i * EMB, i * EMB + 128)
                        pe.matmul(dst, wqkvA[:, col], h0tA[:, tok], start=True, stop=False)
                        ins = pe.matmul(dst, wqkvB[:, col], h0tB[:, tok], start=False, stop=True)
                    else:
                        for im in range(2):
                            tok = slice(im * TOK, (im + 1) * TOK)
                            col = slice(64 - 64 * im, 192 - 64 * im)
                            pe.matmul(dst, wcA[:, i, col], h0tA[:, tok], start=(im == 0), stop=False)
                            ins = pe.matmul(dst, wcB[:, i, col], h0tB[:, tok], start=False, stop=(im == 1))
                ma_done(ins, qk_ok, GROUPS * k + g + 1)

            def values(k, g):
                ma_wait()
                for hf in range(2):
                    parts = [(g, 0, 128)] if g < 2 else [(0, 128, 64), (1, 128, 64)]
                    at = hf * 128
                    for im, c0, w in parts:
                        tok = slice((2 * im + hf) * BT, (2 * im + hf + 1) * BT)
                        col = slice(2 * EMB + c0, 2 * EMB + c0 + w)
                        pe.matmul(psM[0:BT, at:at + w], h0tA[:, tok], wqkvA[:, col], start=True, stop=False)
                        ins = pe.matmul(psM[0:BT, at:at + w], h0tB[:, tok], wqkvB[:, col], start=False, stop=True)
                        at += w
                ma_done(ins, vz_ok, GROUPS * k + g + 1)

            def scores(k, g, j, d):
                n = n_of(k, g, j) + d
                jj, gg = (j + d) % SLOTS, g + (j + d) // SLOTS
                if jj == 0:
                    pe.wait_ge(qm_ok, GROUPS * k + gg + 1)
                v = n if jj == 0 else n - 2 if jj == 1 else n - 1
                if not isinstance(v, int) or v > 0:
                    pe.wait_ge(s_evac, v)
                for i, t in enumerate(tiles_of(jj)):
                    R = rows_of(t)
                    ins = pe.matmul(psS[jj % 2][0:R, i, :], qm[:].rearrange("p h n -> p (h n)")[:, t * TR:t * TR + R],
                                    qk[:, 1, :], start=True, stop=True)
                ins.then_inc(s_full, 1)

            def p_transposes(k, g, j, d):
                n = n_of(k, g, j) + d
                pe.wait_ge(p_ok, n + 1)
                if not isinstance(n, int) or n > 0:
                    pe.wait_ge(pt_evac, n)
                for i, t in enumerate(tiles_of((j + d) % SLOTS)):
                    R = rows_of(t)
                    for f in range(2):
                        ins = pe.transpose(psT[0:BT, i, f, 0:R], E[0:R, (SLOTS * g + j + d) % 3, i, f * BT:(f + 1) * BT], ident[0:R, 0:R])
                ins.then_inc(pt_full, 1)

            def p_values(k, g):
                pe.wait_ge(pt_evac, n_of(k, g, 0) + SLOTS)
                pe.wait_ge(vz_ok, GROUPS * k + g + 1)
                ma_wait()
                for h in range(GH):
                    for f in range(2):
                        ins = pe.matmul(psM[:, 0:TOK], vz[:, f, h * 128:(h + 1) * 128], Pt[:, f, h * TOK:(h + 1) * TOK],
                                        start=(h == 0 and f == 0), stop=(h == GH - 1 and f == 1))
                ma_done(ins, ot_ok, GROUPS * k + g + 1)

            def project(k):
                pe.wait_ge(ot_ok, GROUPS * k + GROUPS)
                for im in range(2):
                    ma_wait()
                    for hf in range(2):
                        tok = slice(hf * BT, (hf + 1) * BT)
                        dst = psM[0:BT, hf * EMB:(hf + 1) * EMB]
                        half = slice(64 * im, 64 * im + 64)
                        pe.matmul(dst, ot[:, im, tok], wpA[:], start=True, stop=False)
                        ins = pe.matmul(dst, ot[half, 2, tok], wpC[half, :], start=False, stop=True)
                    ma_done(ins, att_ok, 2 * k + im + 1)

            def logits(k):
                pe.wait_ge(h1t_ok, 2 * k + 2)
                ma_wait()
                for b in range(NB):
                    dst = psM[0:BT, b * EX:(b + 1) * EX]
                    pe.matmul(dst, h1tA[:, b * BT:(b + 1) * BT], wgA[:], start=True, stop=False)
                    ins = pe.matmul(dst, h1tB[:, b * BT:(b + 1) * BT], wgB[:], start=False, stop=True)
                ma_done(ins, lg_ok, k + 1)

            def gate_rows(k):
                pe.wait_ge(gates_ok, k + 1)
                ma_wait()
                for b in range(NB):
                    ins = pe.transpose(psM[0:EX, b * BT:(b + 1) * BT], gates[:, b, :], ident[0:BT, 0:BT])
                ma_done(ins, gT_ok, k + 1)

            def gate_spread(k, e):
                pe.wait_ge(gT_ok, k + 1)
                ma_wait()
                ma_done(pe.matmul(psM[:, 0:PT_], sel[:, e, :], gT[:], start=True, stop=True), G_ok, EX * k + e + 1)

            def layer1(k, u):
                e, c = divmod(u, HC)
                if c == 0:
                    pe.wait_ge(xg_ok, EX * k + e + 1)
                v = UNITS * k + u - 1
                if not isinstance(v, int) or v > 0:
                    pe.wait_ge(h_evac, v)
                pe.matmul(psH[u % 2][:], w1A[:, e, c * 128:(c + 1) * 128], xgA[:, e % 2, :], start=True, stop=False)
                pe.matmul(psH[u % 2][:], w1B[:, e, c * 128:(c + 1) * 128], xgB[:, e % 2, :], start=False,
                          stop=True).then_inc(h_full, 1)

            def layer2_bias(k):
                v = 2 * k
                if not isinstance(v, int) or v > 0:
                    pe.wait_ge(y2_evac, v)
                for b in range(NB):
                    pe.matmul(psY[b // 2][0:BT, b % 2, :], gT[:, b * BT:(b + 1) * BT], b2s[:], start=(b % 2 == 0),
                              stop=False, skip_group_check=True)

            def layer2(k, u):
                pe.wait_ge(h_evac, UNITS * k + u + 1)
                for b in range(NB):
                    ins = pe.matmul(psY[b // 2][0:BT, b % 2, :], hs[:, u % 2, b * BT:(b + 1) * BT], w2[:, u, :],
                                    start=False, stop=(u == UNITS - 1), skip_group_check=True)
                ins.then_inc(l2_done, 1)

            pe.wait_ge(w_in, 16 * NLOADS)
            pe.wait_ge(const_ok, 1)
            for c in range(NC):
                pe.matmul(psM[0:1, 0:EMB], lnb_col[:, c:c + 1], w_tok[:, c, :], start=(c == 0), stop=False)
            ma_done(pe.matmul(psM[0:1, 0:EMB], ones_row[0:1, 0:1], tokb_row, start=False, stop=True), cvrow_ok, 1)
            ma_wait()
            ma_done(pe.matmul(psM[0:BT, 0:EMB], ones_row[:], cv_row, start=True, stop=True), cv_ok, 1)
            pe.wait_ge(wtok_ok, 1)
            tok1(0)
            pe.wait_ge(h0_ok, 1)
            transposes(h0, 0, h0t_ok)
            prep(0, 0)
            for j in range(LEAD):
                scores(0, 0, j, 0)

            def slot(k, kk, g, j):
                if g == 2 and j == 0 and pair_ok(kk + 1):
                    tok1(k + 1)
                if j == 2 and has(kk, g, j, -SLOTS):
                    p_values(k if g else k - 1, (g - 1) % GROUPS)
                if has(kk, g, j, -2):
                    p_transposes(k, g, j, -2)
                if has(kk, g, j, LEAD):
                    scores(k, g, j, LEAD)
                if j == 2 and g == 0 and has(kk, g, j, -SLOTS):
                    project(k - 1)
                if j == 3 and has(kk, g, j):
                    values(k, g)
                    if g == 2 and pair_ok(kk + 1):
                        pe.wait_ge(h0_ok, k + 2)
                        transposes(h0, k + 1, h0t_ok)
                    if has(kk, g, j, 4):
                        prep(k if g < 2 else k + 1, (g + 1) % GROUPS)
                if g == 0 and j == 5 and pair_ok(kk - 1):
                    pe.wait_ge(h1_ok, k)
                    transposes(h1, k - 1, h1t_ok)
                    logits(k - 1)
                if g == 1 and j == 0 and pair_ok(kk - 1):
                    gate_rows(k - 1)
                    gate_spread(k - 1, 0)
                    layer2_bias(k - 1)
                    layer1(k - 1, 0)
                kp = 2 if g == 0 else 1
                if pair_ok(kk - kp):
                    for u in units_of(g, j):
                        if u + 1 < UNITS:
                            layer1(k - kp, u + 1)
                        layer2(k - kp, u)
                        if u % HC == 2 and u // HC + 1 < EX:
                            gate_spread(k - kp, u // HC + 1)

            schedule(pe, slot, counts=[(free, NC)], latest=last_take)


NLOADS = 30
NMA = NC + 2 + 2 + GROUPS * 3 + 2 + 2 + 1 + 1 + EX

_INS = ['x', 'L0_tok_W', 'L0_tok_b', 'L0_tok_ln1_w', 'L0_tok_ln1_b', 'L0_tok_ln2_w', 'L0_tok_ln2_b',
        'L0_attn_W_qkv', 'L0_attn_b_qkv', 'L0_attn_W_proj', 'L0_attn_b_proj',
        'L0_ffn_Wg', 'L0_ffn_bg', 'L0_ffn_W1', 'L0_ffn_b1', 'L0_ffn_W2', 'L0_ffn_b2']
_OUTS = [((64, 196, 192), 'float32')]


def kernel(**inputs):
    import numpy as _np
    import concourse.bacc as _bacc
    from concourse import mybir as _mybir
    from concourse.bass_utils import run_bass_kernel_spmd as _run

    nc = _bacc.Bacc("TRN2", target_bir_lowering=False, num_devices=1)
    arrays, args = {}, []
    for name in _INS:
        a = _np.ascontiguousarray(inputs[name])
        arrays[f"in_{name}_dram"] = a
        args.append(nc.dram_tensor(f"in_{name}_dram", a.shape, _mybir.dt.from_np(a.dtype), kind="ExternalInput").ap())
    for i, (shape, dtype) in enumerate(_OUTS):
        dt = _mybir.dt.from_np(_np.dtype(dtype))
        args.append(nc.dram_tensor(f"out_{i}_dram", shape, dt, kind="ExternalOutput").ap())
    vit_kernel(nc, *args)
    r = _run(nc, [arrays], core_ids=[0])
    return r.results[0]["out_0_dram"]
```
